# Optimizing a Trainium2 kernel written in Bass

```python
import numpy as np
import jax
import jax.numpy as jnp

def _softmax(x, axis=-1):
    return jax.nn.softmax(x, axis=axis)

def _gelu(x):
    return jax.nn.gelu(x, approximate=True)

def _silu(x):
    return jax.nn.silu(x)

def _sigmoid(x):
    return jax.nn.sigmoid(x)

def _layernorm(x, axis=-1, eps=1e-05):
    m = jnp.mean(x, axis=axis, keepdims=True)
    v = jnp.var(x, axis=axis, keepdims=True)
    return (x - m) / jnp.sqrt(v + eps)

def _scatter_add(tgt, idx, src, axis=0):
    return tgt.at[idx].add(src)

def _segment_sum(src, seg, n):
    return jax.ops.segment_sum(src, seg, n)
kernel_name = 'mk_dlrm_tower_d1_rec_r8_cd48e0'

def setup_inputs(seed: int=0):
    np.random.seed(seed)
    _w = jnp.asarray

    def _rec_inputs():
        import jax
        import jax.numpy as jnp
        _tk = jax.random.key(seed)
        ids = jnp.stack([jax.random.randint(jax.random.fold_in(_tk, 200 + f), (512,), 0, v, jnp.int32) for f, v in enumerate([12500, 125000, 1250, 1000, 1250, 12500, 1000, 1000, 12500, 1250, 1250, 12500, 1250, 1000, 1000, 1000, 1250, 1000, 12500, 12500, 1250, 12500, 1250, 12500, 1000, 1250])], axis=1)
        tbl_0 = 0.05 * jax.random.normal(jax.random.fold_in(_tk, 500 + 0), (12500, 128), jnp.float32)
        tbl_1 = 0.05 * jax.random.normal(jax.random.fold_in(_tk, 500 + 1), (125000, 128), jnp.float32)
        tbl_2 = 0.05 * jax.random.normal(jax.random.fold_in(_tk, 500 + 2), (1250, 128), jnp.float32)
        tbl_3 = 0.05 * jax.random.normal(jax.random.fold_in(_tk, 500 + 3), (1000, 128), jnp.float32)
        tbl_4 = 0.05 * jax.random.normal(jax.random.fold_in(_tk, 500 + 4), (1250, 128), jnp.float32)
        tbl_5 = 0.05 * jax.random.normal(jax.random.fold_in(_tk, 500 + 5), (12500, 128), jnp.float32)
        tbl_6 = 0.05 * jax.random.normal(jax.random.fold_in(_tk, 500 + 6), (1000, 128), jnp.float32)
        tbl_7 = 0.05 * jax.random.normal(jax.random.fold_in(_tk, 500 + 7), (1000, 128), jnp.float32)
        tbl_8 = 0.05 * jax.random.normal(jax.random.fold_in(_tk, 500 + 8), (12500, 128), jnp.float32)
        tbl_9 = 0.05 * jax.random.normal(jax.random.fold_in(_tk, 500 + 9), (1250, 128), jnp.float32)
        tbl_10 = 0.05 * jax.random.normal(jax.random.fold_in(_tk, 500 + 10), (1250, 128), jnp.float32)
        tbl_11 = 0.05 * jax.random.normal(jax.random.fold_in(_tk, 500 + 11), (12500, 128), jnp.float32)
        tbl_12 = 0.05 * jax.random.normal(jax.random.fold_in(_tk, 500 + 12), (1250, 128), jnp.float32)
        tbl_13 = 0.05 * jax.random.normal(jax.random.fold_in(_tk, 500 + 13), (1000, 128), jnp.float32)
        tbl_14 = 0.05 * jax.random.normal(jax.random.fold_in(_tk, 500 + 14), (1000, 128), jnp.float32)
        tbl_15 = 0.05 * jax.random.normal(jax.random.fold_in(_tk, 500 + 15), (1000, 128), jnp.float32)
        tbl_16 = 0.05 * jax.random.normal(jax.random.fold_in(_tk, 500 + 16), (1250, 128), jnp.float32)
        tbl_17 = 0.05 * jax.random.normal(jax.random.fold_in(_tk, 500 + 17), (1000, 128), jnp.float32)
        tbl_18 = 0.05 * jax.random.normal(jax.random.fold_in(_tk, 500 + 18), (12500, 128), jnp.float32)
        tbl_19 = 0.05 * jax.random.normal(jax.random.fold_in(_tk, 500 + 19), (12500, 128), jnp.float32)
        tbl_20 = 0.05 * jax.random.normal(jax.random.fold_in(_tk, 500 + 20), (1250, 128), jnp.float32)
        tbl_21 = 0.05 * jax.random.normal(jax.random.fold_in(_tk, 500 + 21), (12500, 128), jnp.float32)
        tbl_22 = 0.05 * jax.random.normal(jax.random.fold_in(_tk, 500 + 22), (1250, 128), jnp.float32)
        tbl_23 = 0.05 * jax.random.normal(jax.random.fold_in(_tk, 500 + 23), (12500, 128), jnp.float32)
        tbl_24 = 0.05 * jax.random.normal(jax.random.fold_in(_tk, 500 + 24), (1000, 128), jnp.float32)
        tbl_25 = 0.05 * jax.random.normal(jax.random.fold_in(_tk, 500 + 25), (1250, 128), jnp.float32)
        _rk = jax.random.fold_in(_tk, 7)
        r_dense_features = -0.000520686 + 1.00062 * jax.random.normal(jax.random.fold_in(_rk, 101), (512, 128), jnp.float32)
        W_top1 = 0.0405887 * jax.random.normal(jax.random.fold_in(_tk, 801), (607, 512), jnp.float32)
        W_top2 = 0.0441942 * jax.random.normal(jax.random.fold_in(_tk, 802), (512, 256), jnp.float32)
        W_top3 = 0.0625 * jax.random.normal(jax.random.fold_in(_tk, 803), (256, 1), jnp.float32)
        b_top1 = jnp.zeros((512,), jnp.float32)
        b_top2 = jnp.zeros((256,), jnp.float32)
        return (r_dense_features, ids, tbl_0, tbl_1, tbl_2, tbl_3, tbl_4, tbl_5, tbl_6, tbl_7, tbl_8, tbl_9, tbl_10, tbl_11, tbl_12, tbl_13, tbl_14, tbl_15, tbl_16, tbl_17, tbl_18, tbl_19, tbl_20, tbl_21, tbl_22, tbl_23, tbl_24, tbl_25, W_top1, b_top1, W_top2, b_top2, W_top3)
    r_dense_features, ids, tbl_0, tbl_1, tbl_2, tbl_3, tbl_4, tbl_5, tbl_6, tbl_7, tbl_8, tbl_9, tbl_10, tbl_11, tbl_12, tbl_13, tbl_14, tbl_15, tbl_16, tbl_17, tbl_18, tbl_19, tbl_20, tbl_21, tbl_22, tbl_23, tbl_24, tbl_25, W_top1, b_top1, W_top2, b_top2, W_top3 = _rec_inputs()

    def _L0_rec_setup():
        import jax, jax.numpy as jnp
        import numpy as np
        B, F, D = (2048, 26, 128)
        key = jax.random.key(seed)
        k1, k2 = jax.random.split(key)
        dense_features = jax.random.normal(k1, (B, D), dtype=jnp.float32)
        sparse_values = jax.random.normal(k2, (B, F, D), dtype=jnp.float32)
        return {'dense_features': dense_features, 'sparse_values': sparse_values}
    _L0_rec_all = _L0_rec_setup()
    _L0_rec_in = {k: v for k, v in _L0_rec_all.items() if k in ()}
    del _L0_rec_all
    return {'r_dense_features': r_dense_features, 'ids': ids, 'tbl_0': tbl_0, 'tbl_1': tbl_1, 'tbl_2': tbl_2, 'tbl_3': tbl_3, 'tbl_4': tbl_4, 'tbl_5': tbl_5, 'tbl_6': tbl_6, 'tbl_7': tbl_7, 'tbl_8': tbl_8, 'tbl_9': tbl_9, 'tbl_10': tbl_10, 'tbl_11': tbl_11, 'tbl_12': tbl_12, 'tbl_13': tbl_13, 'tbl_14': tbl_14, 'tbl_15': tbl_15, 'tbl_16': tbl_16, 'tbl_17': tbl_17, 'tbl_18': tbl_18, 'tbl_19': tbl_19, 'tbl_20': tbl_20, 'tbl_21': tbl_21, 'tbl_22': tbl_22, 'tbl_23': tbl_23, 'tbl_24': tbl_24, 'tbl_25': tbl_25, 'W_top1': W_top1, 'b_top1': b_top1, 'W_top2': W_top2, 'b_top2': b_top2, 'W_top3': W_top3}

def reference(r_dense_features, ids, tbl_0, tbl_1, tbl_2, tbl_3, tbl_4, tbl_5, tbl_6, tbl_7, tbl_8, tbl_9, tbl_10, tbl_11, tbl_12, tbl_13, tbl_14, tbl_15, tbl_16, tbl_17, tbl_18, tbl_19, tbl_20, tbl_21, tbl_22, tbl_23, tbl_24, tbl_25, W_top1, b_top1, W_top2, b_top2, W_top3):
    import jax
    import jax.numpy as jnp

    def _L0_rec_ref(dense_features, sparse_values):
        import jax, jax.numpy as jnp
        import numpy as np
        B, F, D = (2048, 26, 128)
        sd = jnp.einsum('bfd,bd->bf', sparse_values, dense_features)
        ss = jnp.einsum('bfd,bgd->bfg', sparse_values, sparse_values)
        iu, ju = jnp.triu_indices(F, k=1)
        pairs = ss[:, iu, ju]
        return jnp.concatenate([dense_features, sd, pairs], axis=1)
    e = jnp.stack([tbl_0[ids[:, 0]], tbl_1[ids[:, 1]], tbl_2[ids[:, 2]], tbl_3[ids[:, 3]], tbl_4[ids[:, 4]], tbl_5[ids[:, 5]], tbl_6[ids[:, 6]], tbl_7[ids[:, 7]], tbl_8[ids[:, 8]], tbl_9[ids[:, 9]], tbl_10[ids[:, 10]], tbl_11[ids[:, 11]], tbl_12[ids[:, 12]], tbl_13[ids[:, 13]], tbl_14[ids[:, 14]], tbl_15[ids[:, 15]], tbl_16[ids[:, 16]], tbl_17[ids[:, 17]], tbl_18[ids[:, 18]], tbl_19[ids[:, 19]], tbl_20[ids[:, 20]], tbl_21[ids[:, 21]], tbl_22[ids[:, 22]], tbl_23[ids[:, 23]], tbl_24[ids[:, 24]], tbl_25[ids[:, 25]]], axis=1)
    z = _L0_rec_ref(r_dense_features, e)
    z = z.reshape(z.shape[0], -1)
    h = jnp.concatenate([z, r_dense_features], axis=1)
    h = jnp.maximum(h @ W_top1 + b_top1, 0.0)
    h = jnp.maximum(h @ W_top2 + b_top2, 0.0)
    y = h @ W_top3
    return y

_drawn_inputs = setup_inputs


def setup_inputs(seed=0):
    import zlib

    import numpy as np

    out = dict(_drawn_inputs(seed))
    spreads = {'b_top1': (0.0, 0.1), 'b_top2': (0.0, 0.1)}
    factors = {}
    for name, (base, spread) in spreads.items():
        noise = np.random.default_rng([zlib.crc32(name.encode()), seed]).standard_normal(out[name].shape)
        drawn = base * np.exp(spread * noise) if base else spread * noise
        out[name] = jnp.asarray(drawn.astype(out[name].dtype))
    for name, factor in factors.items():
        out[name] = (out[name] * factor).astype(out[name].dtype)
    return out
```

```python
from contextlib import ExitStack

import concourse.bass as bass
import numpy as np
from concourse import mybir

ALU = mybir.AluOpType
ACT = mybir.ActivationFunctionType
F32 = mybir.dt.float32
BF16 = mybir.dt.bfloat16
F16 = mybir.dt.float16
I32 = mybir.dt.int32
U32 = mybir.dt.uint32

P = 128
D = 128
BATCH = 512
TILES = BATCH // P
N_TABLES = 26
HOT_TABLES = [3, 6, 7, 13, 14, 15]
GATHERED = [t for t in range(N_TABLES) if t not in HOT_TABLES]
N_HOT = len(HOT_TABLES)
N_GATHERED = len(GATHERED)
SLOTS = N_TABLES + 1
FIRST_GATHERED = 1 + N_HOT
SLOT_FEATURE = [0] + [1 + t for t in HOT_TABLES] + [1 + t for t in GATHERED]

HOT_ROWS = 1000
HOT_CHUNKS = 8
HOT_PARTS = HOT_ROWS // HOT_CHUNKS

SIDE = SLOTS - 1
QUADS = 4
QUAD = 32
GROUPS = P // QUADS
UNITS = 2
UNIT_GROUPS = GROUPS // UNITS
PAIR_CHUNKS = -(-SIDE // QUADS)
LAST_ROWS = (SIDE - QUADS * (PAIR_CHUNKS - 1)) * QUAD
QUAD_CHUNKS = [len(range(k, SIDE, QUADS)) for k in range(QUADS)]

H1, H2 = 512, 256
H1_TILES, H2_TILES = H1 // P, H2 // P

SET = 4
SETS = N_GATHERED // SET
assert N_GATHERED % SET == 0

ORDER = (
    [("hot", 0), ("turn", 0, 0), ("hot", 1), ("turn", 0, 1), ("hot", 2), ("turn", 0, 2), ("hot", 3),
     ("turn", 0, 3), ("hot", 4), ("turn", 0, 4), ("hot", 5), ("turn", 1, 0), ("turn", 1, 1), ("turn", 1, 2),
     ("gram", 0, 0), ("turn", 1, 3), ("gram", 0, 1), ("turn", 1, 4), ("gram", 1, 0), ("mlp1", 0),
     ("gram", 1, 1), ("mlp2", 0), ("turn", 2, 0), ("mlp3", 0), ("mlp1", 1), ("turn", 2, 1), ("turn", 2, 2),
     ("mlp2", 1), ("turn", 2, 3), ("mlp3", 1), ("turn", 2, 4), ("gram", 2, 0), ("gram", 2, 1),
     ("turn", 3, 0), ("turn", 3, 1), ("mlp1", 2), ("turn", 3, 2), ("mlp2", 2), ("turn", 3, 3), ("mlp3", 2),
     ("turn", 3, 4), ("gram", 3, 0), ("gram", 3, 1), ("mlp1", 3), ("mlp2", 3), ("mlp3", 3)]
)


def pair_row(a, b):
    a, b = min(a, b), max(a, b)
    return D + a * (SLOTS - 1) - a * (a - 1) // 2 + (b - a - 1)


def build(nc, dense_t, ids, hot_ids, tables, hot_tables, w1_pairs, w1_dense, w2, w3, b1, b2, ident, hot_row, y):
    with ExitStack() as ctx:
        def sb(name, shape, dt):
            return ctx.enter_context(nc.sbuf_tensor(name, shape, dt))

        def psum(name, shape, dt=F32):
            return ctx.enter_context(nc.psum_tensor(name, shape, dt))

        def sem(name):
            return ctx.enter_context(nc.semaphore(name))

        vec = sb("vec", [P, BATCH, SLOTS], F32)
        rows = sb("rows", [P, TILES, N_GATHERED, D], F32)
        ids_sb = sb("ids_sb", [P, TILES, N_GATHERED], I32)
        hot_ids_sb = sb("hot_ids_sb", [HOT_PARTS, N_HOT, BATCH], I32)
        hot_ids_f = sb("hot_ids_f", [HOT_PARTS, 2, BATCH], F16)
        one_hot = sb("one_hot", [HOT_PARTS, 2, HOT_CHUNKS, BATCH], BF16)
        table = sb("table", [HOT_PARTS, 3, HOT_CHUNKS * D], F32)
        rest1 = sb("rest1", [HOT_PARTS, 2, HOT_CHUNKS * D], F32)
        rest2 = sb("rest2", [HOT_PARTS, 2, HOT_CHUNKS * D], F32)
        pair = sb("pair", [P, 2, PAIR_CHUNKS, P], F32)
        dense_sb = sb("dense_sb", [P, BATCH], F32)
        w1p = sb("w1p", [P, PAIR_CHUNKS, H1], F32)
        w1d = sb("w1d", [P, 2, H1], F32)
        w1s = sb("w1s", [P, H1], F32)
        w2_sb = sb("w2_sb", [P, H1_TILES, H2], F32)
        small = sb("small", [P, H2_TILES + H1_TILES + H2_TILES], F32)
        w3_sb = small[:, 0:H2_TILES]
        b1_sb = small[:, H2_TILES:H2_TILES + H1_TILES]
        b2_sb = small[:, H2_TILES + H1_TILES:]
        ident_sb = sb("ident_sb", [P, P], F32)
        hot_row_sb = sb("hot_row_sb", [P, HOT_CHUNKS], F32)
        h1_sb = sb("h1_sb", [P, 2, H1_TILES, P], F32)
        h2_sb = sb("h2_sb", [P, 2, H2_TILES, P], F32)
        y_sb = sb("y_sb", [1, BATCH], F32)

        turn_ps = psum("turn_ps", [P, 2, SET, P])
        hot_ps = psum("hot_ps", [P, BATCH])
        gram_ps = psum("gram_ps", [P, 2, 512])
        h1_ps = psum("h1_ps", [P, 2, 512])
        h2_ps = psum("h2_ps", [P, 512])

        ids_in = sem("ids_in")
        hot_ids_in = sem("hot_ids_in")
        table_in = [sem(f"table_in{i}") for i in range(N_HOT)]
        consts_in = sem("consts_in")
        dense_in = sem("dense_in")
        w1d_in = sem("w1d_in")
        w1p_in = sem("w1p_in")
        mlp_in = sem("mlp_in")
        rows_in = [[sem(f"rows_in{t}_{q}") for q in range(SETS)] for t in range(TILES)]
        zeroed = sem("zeroed")
        dense_set = sem("dense_set")
        w1_summed = sem("w1_summed")
        ids_cast = sem("ids_cast")
        hot_ready = sem("hot_ready")
        rest1_ready = sem("rest1_ready")
        rest2_ready = sem("rest2_ready")
        hot_done = sem("hot_done")
        hot_out = sem("hot_out")
        turn_done = sem("turn_done")
        turn_out = sem("turn_out")
        gram_done = sem("gram_done")
        act_pairs = sem("act_pairs")
        dve_pairs = sem("dve_pairs")
        mlp1_done = sem("mlp1_done")
        act_h1 = sem("act_h1")
        dve_h1 = sem("dve_h1")
        mlp2_done = sem("mlp2_done")
        act_h2 = sem("act_h2")
        dve_h2 = sem("dve_h2")
        mlp3_done = sem("mlp3_done")
        y_set = sem("y_set")
        y_stored = sem("y_stored")

        def sample_slots(t):
            return vec[:, t * P:(t + 1) * P, :].rearrange("d (j g) s -> d j g s", j=QUADS)

        def h1_tile(m):
            return h1_ps[:, m // 2, (m % 2) * P:(m % 2 + 1) * P]

        def h2_tile(m):
            return (h2_ps, hot_ps)[m][:, 0:P]

        def gram_slot(t, u):
            return (t * UNITS + u) % 2

        def pair_copy(copy, t, u, j, k):
            n = QUAD_CHUNKS[k]
            src = gram_ps[QUAD * j:QUAD * j + SIDE, gram_slot(t, u), 0:UNIT_GROUPS * SIDE]
            src = src.rearrange("f (g r) -> f r g", r=SIDE)[:, k:SIDE:QUADS, :]
            at = j * GROUPS + u * UNIT_GROUPS
            return copy(pair[QUAD * k:QUAD * k + SIDE, t % 2, 0:n, at:at + UNIT_GROUPS], src)

        block = ctx.enter_context(nc.Block())

        @block.sync
        def _(sp):
            sp.dma_start(ids_sb[:, :, :], ids).then_inc(ids_in, 16)
            sp.dma_start(hot_ids_sb[:, :, :], hot_ids.partition_broadcast(HOT_PARTS)).then_inc(hot_ids_in, 16)
            for i in range(N_HOT):
                if i >= 3:
                    sp.wait_ge(hot_done, i - 2)
                    sp.wait_ge(rest1_ready, i - 2)
                sp.dma_start(table[:, i % 3, :], hot_tables[i].rearrange("(p c) d -> p (c d)", c=HOT_CHUNKS)
                             ).then_inc(table_in[i], 16)
                if i == 2:
                    sp.dma_start(dense_sb[:, :], dense_t).then_inc(dense_in, 16)
                    sp.dma_start(w1d[:, :, :], w1_dense).then_inc(w1d_in, 16)
                    sp.dma_start(w1p[:, :, :], w1_pairs).then_inc(w1p_in, 16)
                    sp.dma_start(w2_sb[:, :, :], w2.rearrange("(c p) m -> p c m", p=P)).then_inc(mlp_in, 16)
                    sp.dma_start(small[:, 0:H2_TILES], w3).then_inc(mlp_in, 16)
                    sp.dma_start(small[:, H2_TILES:H2_TILES + H1_TILES], b1).then_inc(mlp_in, 16)
                    sp.dma_start(small[:, H2_TILES + H1_TILES:], b2).then_inc(mlp_in, 16)
            sp.wait_ge(y_set, TILES)
            sp.dma_start(y, y_sb[:, :]).then_inc(y_stored, 16)
            sp.wait_ge(y_stored, 16)

        @block.gpsimd
        def _(pool):
            pool.wait_ge(ids_in, 16)
            for t in range(TILES):
                for n in range(N_GATHERED):
                    pool.indirect_dma_start(
                        rows[:, t, n, :], None, tables[n],
                        bass.IndirectOffsetOnAxis(ids_sb[:, t, n:n + 1].bitcast(U32), 0),
                    ).then_inc(rows_in[t][n // SET], 16)

        @block.tensor
        def _(pe):
            def hot(i):
                pe.wait_ge(hot_ready, i + 1)
                pe.wait_ge(table_in[i], 16)
                if i:
                    pe.wait_ge(hot_out, i)
                parts = [table[:, i % 3], rest1[:, i % 2], rest2[:, i % 2]]
                ready = [None, rest1_ready, rest2_ready]
                for n in range(3):
                    if ready[n] is not None:
                        pe.wait_ge(ready[n], i + 1)
                    high = parts[n].bitcast(BF16).rearrange("p (c d h) -> p c d h", d=D, h=2)[:, :, :, 1]
                    for c in range(HOT_CHUNKS):
                        mm = pe.matmul(hot_ps[:, :], high[:, c, :], one_hot[:, i % 2, c, :],
                                       start=(n == 0 and c == 0), stop=(n == 2 and c == HOT_CHUNKS - 1))
                mm.then_inc(hot_done, 1)

            def turn(t, q):
                at = t * SETS + q
                if at == 0:
                    pe.wait_ge(consts_in, 32)
                pe.wait_ge(rows_in[t][q], 16 * SET)
                if at >= 2:
                    pe.wait_ge(turn_out, at - 1)
                for n in range(SET):
                    mm = pe.transpose(turn_ps[:, at % 2, n, :], rows[:, t, q * SET + n, :], ident_sb[:, :])
                mm.then_inc(turn_done, 1)

            def gram(t, u):
                at = t * UNITS + u
                pe.wait_ge(turn_out, (t + 1) * SETS)
                pe.wait_ge(hot_out, N_HOT)
                pe.wait_ge(dense_set, 1)
                if at >= 2:
                    pe.wait_ge(act_pairs, at - 1)
                    pe.wait_ge(dve_pairs, at - 1)
                of = sample_slots(t)
                for g in range(UNIT_GROUPS):
                    for j in range(QUADS):
                        own = of[:, j, u * UNIT_GROUPS + g, :]
                        mm = pe.matmul(gram_ps[QUAD * j:QUAD * j + SIDE, at % 2, g * SIDE:(g + 1) * SIDE],
                                       own[:, 0:SIDE], own[:, 1:SLOTS], start=True, stop=True)
                mm.then_inc(gram_done, 1)

            def mlp1(t):
                if t == 0:
                    pe.wait_ge(w1_summed, 1)
                    pe.wait_ge(w1p_in, 16)
                else:
                    pe.wait_ge(act_h1, t)
                    pe.wait_ge(dve_h1, t)
                pe.wait_ge(act_pairs, UNITS * (t + 1))
                pe.wait_ge(dve_pairs, UNITS * (t + 1))
                for m in range(H1_TILES):
                    cols = slice(m * P, (m + 1) * P)
                    pe.matmul(h1_tile(m), w1s[:, cols], dense_sb[:, t * P:(t + 1) * P], start=True, stop=False)
                    for c in range(PAIR_CHUNKS):
                        k = P if c < PAIR_CHUNKS - 1 else LAST_ROWS
                        mm = pe.matmul(h1_tile(m), w1p[0:k, c, cols], pair[0:k, t % 2, c, :],
                                       start=False, stop=(c == PAIR_CHUNKS - 1))
                mm.then_inc(mlp1_done, 1)

            def mlp2(t):
                if t == 0:
                    pe.wait_ge(mlp_in, 64)
                else:
                    pe.wait_ge(act_h2, t)
                    pe.wait_ge(dve_h2, t)
                    pe.wait_ge(y_set, t)
                pe.wait_ge(act_h1, t + 1)
                pe.wait_ge(dve_h1, t + 1)
                for m in range(H2_TILES):
                    for c in range(H1_TILES):
                        mm = pe.matmul(h2_tile(m), w2_sb[:, c, m * P:(m + 1) * P],
                                       h1_sb[:, t % 2, c, :], start=(c == 0), stop=(c == H1_TILES - 1))
                mm.then_inc(mlp2_done, 1)

            def mlp3(t):
                pe.wait_ge(act_h2, t + 1)
                pe.wait_ge(dve_h2, t + 1)
                if t:
                    pe.wait_ge(y_set, t)
                for c in range(H2_TILES):
                    mm = pe.matmul(h2_ps[0:1, P:2 * P], w3_sb[:, c:c + 1], h2_sb[:, t % 2, c, :],
                                   start=(c == 0), stop=(c == H2_TILES - 1))
                mm.then_inc(mlp3_done, 1)

            steps = {"hot": hot, "turn": turn, "gram": gram, "mlp1": mlp1, "mlp2": mlp2, "mlp3": mlp3}
            for name, *args in ORDER:
                steps[name](*args)

        @block.scalar
        def _(act):
            act.dma_start(ident_sb[:, :], ident).then_inc(consts_in, 16)
            act.dma_start(hot_row_sb[:, :], hot_row).then_inc(consts_in, 16)

            def hot(i):
                act.wait_ge(hot_done, i + 1)
                act.copy(vec[:, :, 1 + i], hot_ps[:, :]).then_inc(hot_out, 1)

            def turn(t, q):
                at = t * SETS + q
                slot = FIRST_GATHERED + q * SET
                act.wait_ge(turn_done, at + 1)
                act.copy(vec[:, t * P:(t + 1) * P, slot:slot + SET],
                         turn_ps[:, at % 2, :, :].rearrange("d n b -> d b n")).then_inc(turn_out, 1)

            def gram(t, u):
                at = t * UNITS + u
                act.wait_ge(gram_done, at + 1)
                if at == 0:
                    act.wait_ge(zeroed, 1)
                if t >= 2:
                    act.wait_ge(mlp1_done, t - 1)
                for j in (0, 1):
                    for k in range(QUADS):
                        last = pair_copy(act.copy, t, u, j, k)
                last.then_inc(act_pairs, 1)

            def mlp1(t):
                act.wait_ge(mlp1_done, t + 1)
                if t == 0:
                    act.wait_ge(mlp_in, 64)
                if t >= 2:
                    act.wait_ge(mlp2_done, t - 1)
                for m in (0, 1):
                    last = act.activation(h1_sb[:, t % 2, m, :], h1_tile(m), ACT.Relu, bias=b1_sb[:, m:m + 1])
                last.then_inc(act_h1, 1)

            def mlp2(t):
                act.wait_ge(mlp2_done, t + 1)
                if t >= 2:
                    act.wait_ge(mlp3_done, t - 1)
                act.activation(h2_sb[:, t % 2, 0, :], h2_tile(0), ACT.Relu, bias=b2_sb[:, 0:1]).then_inc(act_h2, 1)

            def mlp3(t):
                act.wait_ge(mlp3_done, t + 1)
                act.copy(y_sb[:, t * P:(t + 1) * P], h2_ps[0:1, P:2 * P]).then_inc(y_set, 1)

            steps = {"hot": hot, "turn": turn, "gram": gram, "mlp1": mlp1, "mlp2": mlp2, "mlp3": mlp3}
            for name, *args in ORDER:
                steps[name](*args)

        @block.vector
        def _(dve):
            dve.memset(pair[:, :, :, :], 0.0).then_inc(zeroed, 1)

            def prepare_hot(i):
                if i == 0:
                    dve.wait_ge(hot_ids_in, 16)
                    dve.wait_ge(consts_in, 32)
                if i >= 2:
                    dve.wait_ge(hot_done, i - 1)
                dve.tensor_copy(hot_ids_f[:, i % 2, :], hot_ids_sb[:, i, :]).then_inc(ids_cast, 1)
                dve.wait_ge(ids_cast, i + 1)
                for c in range(HOT_CHUNKS):
                    last = dve.tensor_scalar(one_hot[:, i % 2, c, :], hot_ids_f[:, i % 2, :],
                                             hot_row_sb[0:HOT_PARTS, c:c + 1], None, ALU.is_equal)
                last.then_inc(hot_ready, 1)
                dve.wait_ge(table_in[i], 16)
                dve.tensor_tensor(rest1[:, i % 2, :], table[:, i % 3, :], high_half(table[:, i % 3, :]),
                                  ALU.subtract).then_inc(rest1_ready, 1)
                dve.wait_ge(rest1_ready, i + 1)
                dve.tensor_tensor(rest2[:, i % 2, :], rest1[:, i % 2, :], high_half(rest1[:, i % 2, :]),
                                  ALU.subtract).then_inc(rest2_ready, 1)

            def high_half(x):
                return x.bitcast(BF16).rearrange("p (n h) -> p n h", h=2)[:, :, 1]

            def hot(i):
                if i + 2 < N_HOT:
                    prepare_hot(i + 2)
                if i == 1:
                    dve.wait_ge(dense_in, 16)
                    dve.tensor_copy(vec[:, :, 0], dense_sb[:, :]).then_inc(dense_set, 1)
                    dve.wait_ge(w1d_in, 16)
                    dve.tensor_tensor(w1s[:, :], w1d[:, 0, :], w1d[:, 1, :], ALU.add).then_inc(w1_summed, 1)

            def turn(t, q):
                pass

            def gram(t, u):
                at = t * UNITS + u
                dve.wait_ge(gram_done, at + 1)
                if at == 0:
                    dve.wait_ge(zeroed, 1)
                if t >= 2:
                    dve.wait_ge(mlp1_done, t - 1)
                for j in (2, 3):
                    for k in range(QUADS):
                        last = pair_copy(dve.tensor_copy, t, u, j, k)
                last.then_inc(dve_pairs, 1)

            def mlp1(t):
                dve.wait_ge(mlp1_done, t + 1)
                if t == 0:
                    dve.wait_ge(mlp_in, 64)
                if t >= 2:
                    dve.wait_ge(mlp2_done, t - 1)
                for m in (2, 3):
                    last = dve.tensor_scalar(h1_sb[:, t % 2, m, :], h1_tile(m), b1_sb[:, m:m + 1], 0.0,
                                             ALU.add, ALU.max)
                last.then_inc(dve_h1, 1)

            def mlp2(t):
                dve.wait_ge(mlp2_done, t + 1)
                if t >= 2:
                    dve.wait_ge(mlp3_done, t - 1)
                dve.tensor_scalar(h2_sb[:, t % 2, 1, :], h2_tile(1), b2_sb[:, 1:2], 0.0,
                                  ALU.add, ALU.max).then_inc(dve_h2, 1)

            def mlp3(t):
                pass

            prepare_hot(0)
            prepare_hot(1)
            steps = {"hot": hot, "turn": turn, "gram": gram, "mlp1": mlp1, "mlp2": mlp2, "mlp3": mlp3}
            for name, *args in ORDER:
                steps[name](*args)


def kernel(**inputs):
    import concourse.bacc as bacc
    from concourse.bass_utils import run_bass_kernel_spmd

    a = {k: np.asarray(v) for k, v in inputs.items()}
    w1 = a["W_top1"]
    w1_pairs = np.zeros((P, PAIR_CHUNKS, H1), np.float32)
    for right in range(1, SLOTS):
        c, k = divmod(right - 1, QUADS)
        for left in range(right):
            w1_pairs[k * QUAD + left, c] = w1[pair_row(SLOT_FEATURE[left], SLOT_FEATURE[right])]
    ids = a["ids"].reshape(TILES, P, N_TABLES)
    arrays = {
        "dense_t": a["r_dense_features"].T,
        "ids": ids[:, :, GATHERED].transpose(1, 0, 2),
        "hot_ids": a["ids"][:, HOT_TABLES].T,
        "w1_pairs": w1_pairs,
        "w1_dense": np.stack([w1[0:D], w1[-D:]], axis=1),
        "w2": a["W_top2"],
        "w3": a["W_top3"].reshape(H2_TILES, P).T,
        "b1": a["b_top1"].reshape(H1_TILES, P).T,
        "b2": a["b_top2"].reshape(H2_TILES, P).T,
        "ident": np.eye(P, dtype=np.float32),
        "hot_row": np.arange(P * HOT_CHUNKS, dtype=np.float32).reshape(P, HOT_CHUNKS),
    }
    arrays |= {f"tbl_{t}": a[f"tbl_{t}"] for t in range(N_TABLES)}
    arrays = {k: np.ascontiguousarray(v) for k, v in arrays.items()}

    nc = bacc.Bacc("TRN2", target_bir_lowering=False, num_devices=1)
    aps = {k: nc.dram_tensor(k, v.shape, mybir.dt.from_np(v.dtype), kind="ExternalInput").ap()
           for k, v in arrays.items()}
    y = nc.dram_tensor("y", (BATCH, 1), F32, kind="ExternalOutput").ap()
    build(nc, aps["dense_t"], aps["ids"], aps["hot_ids"], [aps[f"tbl_{t}"] for t in GATHERED],
          [aps[f"tbl_{t}"] for t in HOT_TABLES], aps["w1_pairs"], aps["w1_dense"], aps["w2"], aps["w3"],
          aps["b1"], aps["b2"], aps["ident"], aps["hot_row"], y.rearrange("b o -> o b"))
    r = run_bass_kernel_spmd(nc, [arrays], core_ids=[0])
    return r.results[0]["y"]
```

```python
from contextlib import ExitStack

import concourse.bass as bass
import numpy as np
from concourse import mybir

ALU = mybir.AluOpType
ACT = mybir.ActivationFunctionType
F32 = mybir.dt.float32
BF16 = mybir.dt.bfloat16
F16 = mybir.dt.float16
I32 = mybir.dt.int32
U32 = mybir.dt.uint32

P = 128
D = 128
BATCH = 512
TILES = BATCH // P
N_TABLES = 26
HOT_TABLES = [3, 6, 7, 13, 14, 15]
GATHERED = [t for t in range(N_TABLES) if t not in HOT_TABLES]
N_HOT = len(HOT_TABLES)
N_GATHERED = len(GATHERED)
SLOTS = N_TABLES + 1
FIRST_GATHERED = 1 + N_HOT
SLOT_FEATURE = [0] + [1 + t for t in HOT_TABLES] + [1 + t for t in GATHERED]

HOT_ROWS = 1000
HOT_CHUNKS = 8
HOT_PARTS = HOT_ROWS // HOT_CHUNKS

SIDE = SLOTS - 1
QUADS = 4
QUAD = 32
GROUPS = P // QUADS
UNITS = 2
UNIT_GROUPS = GROUPS // UNITS
PAIR_CHUNKS = -(-SIDE // QUADS)
HALF = SIDE // 2
WIDE_ROWS = HALF * SIDE
LIST_ROWS = WIDE_ROWS + HALF * HALF
LIST_CHUNKS = -(-LIST_ROWS // P)
LIST_LAST = LIST_ROWS - P * (LIST_CHUNKS - 1)
LAST = TILES - 1
FIRST_DIRECT = 2
LAST_ROWS = (SIDE - QUADS * (PAIR_CHUNKS - 1)) * QUAD
QUAD_CHUNKS = [len(range(k, SIDE, QUADS)) for k in range(QUADS)]

H1, H2 = 512, 256
WARM_UP = 10
H1_TILES, H2_TILES = H1 // P, H2 // P

LATE_CHUNK = PAIR_CHUNKS - 2
EARLY_SIDE = LATE_CHUNK * QUADS
N_LATE = SIDE - EARLY_SIDE


def cut(first, end, most=4):
    return [(i, min(i + most, end)) for i in range(first, end, most)]


EARLY_SETS = cut(0, N_GATHERED - N_LATE)
SET_OF = EARLY_SETS + cut(N_GATHERED - N_LATE, N_GATHERED)
SETS = len(SET_OF)

ORDER = [
    ("hot", 0), ("turn", 0, 0), ("hot", 1), ("turn", 0, 1), ("hot", 2), ("turn", 0, 2), ("hot", 3),
    ("turn", 0, 3), ("hot", 4), ("turn", 0, 4), ("turn", 0, 5), ("hot", 5), ("turn", 1, 0), ("turn", 1, 1),
    ("gram", 0, 0), ("gram", 0, 1), ("turn", 1, 2), ("turn", 1, 3), ("turn", 1, 4), ("turn", 1, 5),
    ("gram", 1, 0), ("gram", 1, 1), ("turn", 2, 0), ("mlp1", 0), ("turn", 2, 1), ("turn", 2, 2), ("mlp2", 0),
    ("mlp1", 1), ("mlp3", 0), ("turn", 2, 3), ("turn", 2, 4), ("turn", 2, 5), ("mlp2", 1), ("gram", 2, 0),
    ("gram", 2, 1), ("mlp3", 1), ("turn", 3, 0), ("mlp1", 2), ("turn", 3, 1), ("turn", 3, 2), ("turn", 3, 3), ("mlp2", 2),
    ("early", 0), ("early", 1), ("turn", 3, 4), ("turn", 3, 5), ("mlp3", 2), ("late", 0), ("late", 1), ("mlp1_early",),
    ("mlp1_late",), ("mlp2", 3), ("mlp3", 3),
]


def pair_row(a, b):
    a, b = min(a, b), max(a, b)
    return D + a * (SLOTS - 1) - a * (a - 1) // 2 + (b - a - 1)


def list_row(left, right):
    if left < HALF:
        return left * SIDE + right
    return WIDE_ROWS + (left - HALF) * HALF + right - HALF


def build(nc, dense_t, ids, hot_ids, tables, hot_tables, w1_pairs, w1_list, w1_dense, w2, w3, b1, b2, ident, hot_row, gram_dram, y):
    with ExitStack() as ctx:
        def sb(name, shape, dt):
            return ctx.enter_context(nc.sbuf_tensor(name, shape, dt))

        def psum(name, shape, dt=F32):
            return ctx.enter_context(nc.psum_tensor(name, shape, dt))

        def sem(name):
            return ctx.enter_context(nc.semaphore(name))

        vec = sb("vec", [P, BATCH, SLOTS], F32)
        rows = sb("rows", [P, 2, N_GATHERED, D], F32)
        ids_sb = sb("ids_sb", [P, TILES, N_GATHERED], I32)
        hot_ids_sb = sb("hot_ids_sb", [HOT_PARTS, 2, BATCH], I32)
        hot_ids_f = sb("hot_ids_f", [HOT_PARTS, 2, BATCH], F16)
        one_hot = sb("one_hot", [HOT_PARTS, 2, HOT_CHUNKS, BATCH], BF16)
        table = sb("table", [HOT_PARTS, 3, HOT_CHUNKS * D], F32)
        rest1 = sb("rest1", [HOT_PARTS, 2, HOT_CHUNKS * D], F32)
        rest2 = sb("rest2", [HOT_PARTS, 2, HOT_CHUNKS * D], F32)
        gram_sb = sb("gram_sb", [SIDE, 2, SIDE, P], F32)
        listed = sb("listed", [P, 2, LIST_CHUNKS, P], F32)
        pair = sb("pair", [P, 2, PAIR_CHUNKS, P], F32)
        warm = sb("warm", [P, BATCH], BF16)
        dense_sb = sb("dense_sb", [P, BATCH], F32)
        w1p = sb("w1p", [P, PAIR_CHUNKS, H1], F32)
        w1l = sb("w1l", [P, LIST_CHUNKS, H1], F32)
        w1d = sb("w1d", [P, 2, H1], F32)
        w1s = w1d[:, 0, :]
        w2_sb = sb("w2_sb", [P, H1_TILES, H2], F32)
        small = sb("small", [P, H2_TILES + H1_TILES + H2_TILES], F32)
        w3_sb = small[:, 0:H2_TILES]
        b1_sb = small[:, H2_TILES:H2_TILES + H1_TILES]
        b2_sb = small[:, H2_TILES + H1_TILES:]
        ident_sb = sb("ident_sb", [P, P], F32)
        hot_row_sb = sb("hot_row_sb", [P, HOT_CHUNKS], F32)
        h1_sb = sb("h1_sb", [P, 2, H1_TILES, P], F32)
        h2_sb = sb("h2_sb", [P, 2, H2_TILES, P], F32)
        y_sb = sb("y_sb", [1, BATCH], F32)

        turn_ps = psum("turn_ps", [P, 2, 512])
        hot_ps = psum("hot_ps", [P, 2, BATCH])
        gram_ps = psum("gram_ps", [P, 2, 512])
        h1_ps = psum("h1_ps", [P, 2, 512])

        ids_in = sem("ids_in")
        hot_ids_in = [sem(f"hot_ids_in{i}") for i in range(N_HOT)]
        table_in = [sem(f"table_in{i}") for i in range(N_HOT)]
        hot_row_in = sem("hot_row_in")
        ident_in = sem("ident_in")
        dense_in = sem("dense_in")
        w1d_in = sem("w1d_in")
        w1p_in = sem("w1p_in")
        w1l_in = sem("w1l_in")
        grams_stored = [sem(f"grams_stored{t}") for t in range(FIRST_DIRECT)]
        listed_in = [sem(f"listed_in{t}") for t in range(FIRST_DIRECT)]
        mlp_in = sem("mlp_in")
        rows_in = [[sem(f"rows_in{t}_{q}") for q in range(SETS)] for t in range(TILES)]
        zeroed = sem("zeroed")
        warm_set = sem("warm_set")
        dense_set = sem("dense_set")
        w1_summed = sem("w1_summed")
        ids_cast = sem("ids_cast")
        hot_ready = sem("hot_ready")
        rest1_ready = sem("rest1_ready")
        rest2_ready = sem("rest2_ready")
        hot_done = sem("hot_done")
        hot_out = sem("hot_out")
        turn_done = sem("turn_done")
        turn_out = sem("turn_out")
        gram_done = sem("gram_done")
        act_pairs = sem("act_pairs")
        dve_pairs = sem("dve_pairs")
        mlp1_done = sem("mlp1_done")
        act_h1 = sem("act_h1")
        dve_h1 = sem("dve_h1")
        mlp2_done = sem("mlp2_done")
        act_h2 = sem("act_h2")
        dve_h2 = sem("dve_h2")
        mlp3_done = sem("mlp3_done")
        y_set = sem("y_set")
        y_stored = sem("y_stored")

        def sample_slots(t):
            return vec[:, t * P:(t + 1) * P, :].rearrange("d (j g) s -> d j g s", j=QUADS)

        def h1_tile(m):
            return h1_ps[:, m // 2, (m % 2) * P:(m % 2 + 1) * P]

        def h2_tile(m):
            return hot_ps[:, m, 0:P]

        def gram_slot(t, u):
            return (t * UNITS + u) % 2

        def pair_copies(copy, t, u, quads, lefts, first, end):
            for j in quads:
                at = j * GROUPS + u * UNIT_GROUPS
                src = gram_ps[QUAD * j:QUAD * j + lefts, u, 0:UNIT_GROUPS * (end - first)]
                src = src.rearrange("f (g r) -> f r g", r=end - first)
                for k in range(QUADS):
                    n = len(range(first + k, end, QUADS))
                    last = copy(pair[QUAD * k:QUAD * k + lefts, t % 2, first // QUADS:first // QUADS + n,
                                     at:at + UNIT_GROUPS], src[:, k:end - first:QUADS, :])
            return last

        def gram_copy(copy, t, u, j):
            src = gram_ps[QUAD * j:QUAD * j + SIDE, gram_slot(t, u), 0:UNIT_GROUPS * SIDE]
            at = j * GROUPS + u * UNIT_GROUPS
            return copy(gram_sb[:, t % 2, :, at:at + UNIT_GROUPS], src.rearrange("f (g r) -> f r g", r=SIDE))

        block = ctx.enter_context(nc.Block())

        @block.sync
        def _(sp):
            for i in range(N_HOT):
                if i >= 2:
                    sp.wait_ge(ids_cast, i - 1)
                sp.dma_start(hot_ids_sb[:, i % 2, :], hot_ids[i].partition_broadcast(HOT_PARTS)
                             ).then_inc(hot_ids_in[i], 16)
                if i >= 3:
                    sp.wait_ge(hot_done, i - 2)
                    sp.wait_ge(rest1_ready, i - 2)
                sp.dma_start(table[:, i % 3, :], hot_tables[i].rearrange("(p c) d -> p (c d)", c=HOT_CHUNKS)
                             ).then_inc(table_in[i], 16)
                if i == 2:
                    sp.dma_start(dense_sb[:, :], dense_t).then_inc(dense_in, 16)
                    sp.dma_start(w1d[:, :, :], w1_dense).then_inc(w1d_in, 16)
                    sp.dma_start(w1l[:, :, :], w1_list).then_inc(w1l_in, 16)
                    sp.dma_start(w2_sb[:, :, :], w2.rearrange("(c p) m -> p c m", p=P)).then_inc(mlp_in, 16)
                    sp.dma_start(small[:, 0:H2_TILES], w3).then_inc(mlp_in, 16)
                    sp.dma_start(small[:, H2_TILES:H2_TILES + H1_TILES], b1).then_inc(mlp_in, 16)
                    sp.dma_start(small[:, H2_TILES + H1_TILES:], b2).then_inc(mlp_in, 16)
            sp.dma_start(w1p[:, :, :], w1_pairs).then_inc(w1p_in, 16)
            for t in range(FIRST_DIRECT):
                sp.wait_ge(act_pairs, UNITS * (t + 1))
                sp.wait_ge(dve_pairs, UNITS * (t + 1))
                sp.dma_start(gram_dram[t, 0:WIDE_ROWS, :].rearrange("(l r) b -> l r b", r=SIDE),
                             gram_sb[0:HALF, t % 2, :, :]).then_inc(grams_stored[t], 16)
                sp.dma_start(gram_dram[t, WIDE_ROWS:LIST_ROWS, :].rearrange("(l r) b -> l r b", r=HALF),
                             gram_sb[HALF:SIDE, t % 2, HALF:SIDE, :]).then_inc(grams_stored[t], 16)
                if t >= 2:
                    sp.wait_ge(mlp1_done, t - 1)
                sp.wait_ge(grams_stored[t], 32)
                sp.dma_start(listed[:, t % 2, 0:LIST_CHUNKS - 1, :],
                             gram_dram[t, 0:P * (LIST_CHUNKS - 1), :].rearrange("(c p) b -> p c b", p=P)
                             ).then_inc(listed_in[t], 16)
                sp.dma_start(listed[0:LIST_LAST, t % 2, LIST_CHUNKS - 1, :],
                             gram_dram[t, P * (LIST_CHUNKS - 1):LIST_ROWS, :]).then_inc(listed_in[t], 16)
            sp.wait_ge(y_set, TILES)
            sp.dma_start(y, y_sb[:, :]).then_inc(y_stored, 16)
            sp.wait_ge(y_stored, 16)

        @block.gpsimd
        def _(pool):
            pool.wait_ge(ids_in, 16)
            for t in range(TILES):
                for q, (first, end) in enumerate(SET_OF):
                    if t >= 2:
                        pool.wait_ge(turn_done, (t - 2) * SETS + q + 1)
                    for n in range(first, end):
                        pool.indirect_dma_start(
                            rows[:, t % 2, n, :], None, tables[n],
                            bass.IndirectOffsetOnAxis(ids_sb[:, t, n:n + 1].bitcast(U32), 0),
                        ).then_inc(rows_in[t][q], 16)

        @block.tensor
        def _(pe):
            def hot(i):
                pe.wait_ge(table_in[i], 16)
                if i >= 2:
                    pe.wait_ge(hot_out, i - 1)
                parts = [table[:, i % 3], rest1[:, i % 2], rest2[:, i % 2]]
                ready = [None, rest1_ready, rest2_ready]
                for n in range(3):
                    if ready[n] is not None:
                        pe.wait_ge(ready[n], i + 1)
                    high = parts[n].bitcast(BF16).rearrange("p (c d h) -> p c d h", d=D, h=2)[:, :, :, 1]
                    for c in range(HOT_CHUNKS):
                        if n == 0:
                            pe.wait_ge(hot_ready, i * HOT_CHUNKS + c + 1)
                        mm = pe.matmul(hot_ps[:, i % 2, :], high[:, c, :], one_hot[:, i % 2, c, :],
                                       start=(n == 0 and c == 0), stop=(n == 2 and c == HOT_CHUNKS - 1))
                mm.then_inc(hot_done, 1)

            def turn(t, q):
                first, end = SET_OF[q]
                at = t * SETS + q
                if at == 0:
                    pe.wait_ge(ident_in, 16)
                pe.wait_ge(rows_in[t][q], 16 * (end - first))
                if at >= 2:
                    pe.wait_ge(turn_out, at - 1)
                for n in range(first, end):
                    mm = pe.transpose(turn_ps[:, at % 2, (n - first) * P:(n - first + 1) * P], rows[:, t % 2, n, :],
                                      ident_sb[:, :])
                mm.then_inc(turn_done, 1)

            def products(t, u, lefts, first, end):
                at = t * UNITS + u
                n = end - first
                of = sample_slots(t)
                for g in range(UNIT_GROUPS):
                    for j in range(QUADS):
                        own = of[:, j, u * UNIT_GROUPS + g, :]
                        mm = pe.matmul(gram_ps[QUAD * j:QUAD * j + lefts, u, g * n:(g + 1) * n],
                                       own[:, 0:lefts], own[:, 1 + first:1 + end], start=True, stop=True)
                mm.then_inc(gram_done, 1)

            def grams_read(n):
                pe.wait_ge(act_pairs, n)
                pe.wait_ge(dve_pairs, n)

            def gram(t, u):
                pe.wait_ge(turn_out, (t + 1) * SETS)
                if t == 0:
                    pe.wait_ge(hot_out, N_HOT)
                    pe.wait_ge(dense_set, 1)
                else:
                    grams_read(UNITS * (t - 1) + u + 1)
                products(t, u, SIDE, 0, SIDE)

            def early(u):
                pe.wait_ge(turn_out, LAST * SETS + len(EARLY_SETS))
                grams_read(UNITS * (LAST - 1) + u + 1)
                products(LAST, u, EARLY_SIDE, 0, EARLY_SIDE)

            def late(u):
                pe.wait_ge(turn_out, TILES * SETS)
                grams_read(UNITS * LAST + u + 1)
                products(LAST, u, SIDE, EARLY_SIDE, SIDE)

            def add_dense(t):
                if t == 0:
                    pe.wait_ge(w1_summed, 1)
                else:
                    pe.wait_ge(act_h1, t)
                    pe.wait_ge(dve_h1, t)
                for m in range(H1_TILES):
                    pe.matmul(h1_tile(m), w1s[:, m * P:(m + 1) * P], dense_sb[:, t * P:(t + 1) * P],
                              start=(m % 2 == 0), stop=False, skip_group_check=True)

            def add_pairs(weight, value, chunks, last_rows, ends):
                for m in range(H1_TILES):
                    for c in chunks:
                        k = last_rows if c == chunks[-1] else P
                        mm = pe.matmul(h1_tile(m), weight[0:k, c, m * P:(m + 1) * P], value[0:k, c, :], start=False,
                                       stop=(ends and c == chunks[-1]), skip_group_check=True)
                return mm

            def mlp1(t):
                add_dense(t)
                if t < FIRST_DIRECT:
                    if t == 0:
                        pe.wait_ge(w1l_in, 16)
                    pe.wait_ge(listed_in[t], 32)
                    last = add_pairs(w1l, listed[:, t % 2], range(LIST_CHUNKS), LIST_LAST, True)
                else:
                    pe.wait_ge(w1p_in, 16)
                    grams_read(UNITS * (t + 1))
                    last = add_pairs(w1p, pair[:, t % 2], range(PAIR_CHUNKS), LAST_ROWS, True)
                last.then_inc(mlp1_done, 1)

            def mlp1_early():
                add_dense(LAST)
                grams_read(UNITS * (LAST + 1))
                add_pairs(w1p, pair[:, LAST % 2], range(LATE_CHUNK), P, False)

            def mlp1_late():
                grams_read(UNITS * (LAST + 2))
                add_pairs(w1p, pair[:, LAST % 2], range(LATE_CHUNK, PAIR_CHUNKS), LAST_ROWS, True
                          ).then_inc(mlp1_done, 1)

            def mlp2(t):
                if t == 0:
                    pe.wait_ge(mlp_in, 64)
                else:
                    pe.wait_ge(act_h2, t)
                    pe.wait_ge(dve_h2, t)
                    pe.wait_ge(y_set, t)
                pe.wait_ge(act_h1, t + 1)
                pe.wait_ge(dve_h1, t + 1)
                for m in range(H2_TILES):
                    for c in range(H1_TILES):
                        mm = pe.matmul(h2_tile(m), w2_sb[:, c, m * P:(m + 1) * P],
                                       h1_sb[:, t % 2, c, :], start=(c == 0), stop=(c == H1_TILES - 1))
                mm.then_inc(mlp2_done, 1)

            def mlp3(t):
                pe.wait_ge(act_h2, t + 1)
                pe.wait_ge(dve_h2, t + 1)
                if t:
                    pe.wait_ge(y_set, t)
                for c in range(H2_TILES):
                    mm = pe.matmul(hot_ps[0:1, 0, P:2 * P], w3_sb[:, c:c + 1], h2_sb[:, t % 2, c, :],
                                   start=(c == 0), stop=(c == H2_TILES - 1))
                mm.then_inc(mlp3_done, 1)

            pe.wait_ge(warm_set, 1)
            for _ in range(WARM_UP):
                pe.matmul(hot_ps[:, 1, :], warm[:, 0:P], warm[:, :], start=True, stop=True)
            steps = {"hot": hot, "turn": turn, "gram": gram, "early": early, "late": late, "mlp1": mlp1,
                     "mlp1_early": mlp1_early, "mlp1_late": mlp1_late, "mlp2": mlp2, "mlp3": mlp3}
            for name, *args in ORDER:
                steps[name](*args)

        @block.scalar
        def _(act):
            act.dma_start(ids_sb[:, :, :], ids).then_inc(ids_in, 16)
            act.dma_start(hot_row_sb[:, :], hot_row).then_inc(hot_row_in, 16)
            act.dma_start(ident_sb[:, :], ident).then_inc(ident_in, 16)

            def hot(i):
                act.wait_ge(hot_done, i + 1)
                act.copy(vec[:, :, 1 + i], hot_ps[:, i % 2, :]).then_inc(hot_out, 1)

            def turn(t, q):
                at = t * SETS + q
                first, end = SET_OF[q]
                act.wait_ge(turn_done, at + 1)
                act.copy(vec[:, t * P:(t + 1) * P, FIRST_GATHERED + first:FIRST_GATHERED + end],
                         turn_ps[:, at % 2, 0:(end - first) * P].rearrange("d (n b) -> d b n", b=P)
                         ).then_inc(turn_out, 1)

            def gram(t, u):
                act.wait_ge(gram_done, t * UNITS + u + 1)
                if t >= FIRST_DIRECT:
                    act.wait_ge(zeroed, 1)
                    last = pair_copies(act.copy, t, u, (0, 1), SIDE, 0, SIDE)
                else:
                    for j in (0, 1):
                        last = gram_copy(act.copy, t, u, j)
                last.then_inc(act_pairs, 1)

            def early(u):
                act.wait_ge(gram_done, UNITS * LAST + u + 1)
                pair_copies(act.copy, LAST, u, (0, 1), EARLY_SIDE, 0, EARLY_SIDE).then_inc(act_pairs, 1)

            def late(u):
                act.wait_ge(gram_done, UNITS * (LAST + 1) + u + 1)
                pair_copies(act.copy, LAST, u, (0, 1), SIDE, EARLY_SIDE, SIDE).then_inc(act_pairs, 1)

            def mlp1(t):
                act.wait_ge(mlp1_done, t + 1)
                if t == 0:
                    act.wait_ge(mlp_in, 64)
                if t >= 2:
                    act.wait_ge(mlp2_done, t - 1)
                for m in (0, 1):
                    last = act.activation(h1_sb[:, t % 2, m, :], h1_tile(m), ACT.Relu, bias=b1_sb[:, m:m + 1])
                last.then_inc(act_h1, 1)

            def mlp1_early():
                pass

            def mlp1_late():
                mlp1(LAST)

            def mlp2(t):
                act.wait_ge(mlp2_done, t + 1)
                if t >= 2:
                    act.wait_ge(mlp3_done, t - 1)
                act.activation(h2_sb[:, t % 2, 0, :], h2_tile(0), ACT.Relu, bias=b2_sb[:, 0:1]).then_inc(act_h2, 1)

            def mlp3(t):
                act.wait_ge(mlp3_done, t + 1)
                act.copy(y_sb[:, t * P:(t + 1) * P], hot_ps[0:1, 0, P:2 * P]).then_inc(y_set, 1)

            steps = {"hot": hot, "turn": turn, "gram": gram, "early": early, "late": late, "mlp1": mlp1,
                     "mlp1_early": mlp1_early, "mlp1_late": mlp1_late, "mlp2": mlp2, "mlp3": mlp3}
            for name, *args in ORDER:
                steps[name](*args)

        @block.vector
        def _(dve):

            def prepare_hot(i):
                if i == 0:
                    dve.wait_ge(hot_row_in, 16)
                dve.wait_ge(hot_ids_in[i], 16)
                if i >= 2:
                    dve.wait_ge(hot_done, i - 1)
                dve.tensor_copy(hot_ids_f[:, i % 2, :], hot_ids_sb[:, i % 2, :]).then_inc(ids_cast, 1)
                dve.wait_ge(ids_cast, i + 1)
                for c in range(HOT_CHUNKS):
                    dve.tensor_scalar(one_hot[:, i % 2, c, :], hot_ids_f[:, i % 2, :],
                                      hot_row_sb[0:HOT_PARTS, c:c + 1], None, ALU.is_equal).then_inc(hot_ready, 1)
                dve.wait_ge(table_in[i], 16)
                dve.tensor_tensor(rest1[:, i % 2, :], table[:, i % 3, :], high_half(table[:, i % 3, :]),
                                  ALU.subtract).then_inc(rest1_ready, 1)
                dve.wait_ge(rest1_ready, i + 1)
                dve.tensor_tensor(rest2[:, i % 2, :], rest1[:, i % 2, :], high_half(rest1[:, i % 2, :]),
                                  ALU.subtract).then_inc(rest2_ready, 1)

            def high_half(x):
                return x.bitcast(BF16).rearrange("p (n h) -> p n h", h=2)[:, :, 1]

            def hot(i):
                if i + 2 < N_HOT:
                    prepare_hot(i + 2)
                if i == 1:
                    dve.wait_ge(dense_in, 16)
                    dve.tensor_copy(vec[:, :, 0], dense_sb[:, :]).then_inc(dense_set, 1)
                    dve.wait_ge(w1d_in, 16)
                    dve.tensor_tensor(w1s[:, :], w1d[:, 0, :], w1d[:, 1, :], ALU.add).then_inc(w1_summed, 1)

            def turn(t, q):
                pass

            def gram(t, u):
                dve.wait_ge(gram_done, t * UNITS + u + 1)
                if t >= FIRST_DIRECT:
                    dve.wait_ge(zeroed, 1)
                    last = pair_copies(dve.tensor_copy, t, u, (2, 3), SIDE, 0, SIDE)
                else:
                    for j in (2, 3):
                        last = gram_copy(dve.tensor_copy, t, u, j)
                last.then_inc(dve_pairs, 1)

            def early(u):
                dve.wait_ge(gram_done, UNITS * LAST + u + 1)
                pair_copies(dve.tensor_copy, LAST, u, (2, 3), EARLY_SIDE, 0, EARLY_SIDE).then_inc(dve_pairs, 1)

            def late(u):
                dve.wait_ge(gram_done, UNITS * (LAST + 1) + u + 1)
                pair_copies(dve.tensor_copy, LAST, u, (2, 3), SIDE, EARLY_SIDE, SIDE).then_inc(dve_pairs, 1)

            def mlp1(t):
                dve.wait_ge(mlp1_done, t + 1)
                if t == 0:
                    dve.wait_ge(mlp_in, 64)
                if t >= 2:
                    dve.wait_ge(mlp2_done, t - 1)
                for m in (2, 3):
                    last = dve.tensor_scalar(h1_sb[:, t % 2, m, :], h1_tile(m), b1_sb[:, m:m + 1], 0.0,
                                             ALU.add, ALU.max)
                last.then_inc(dve_h1, 1)

            def mlp1_early():
                pass

            def mlp1_late():
                mlp1(LAST)

            def mlp2(t):
                dve.wait_ge(mlp2_done, t + 1)
                if t >= 2:
                    dve.wait_ge(mlp3_done, t - 1)
                dve.tensor_scalar(h2_sb[:, t % 2, 1, :], h2_tile(1), b2_sb[:, 1:2], 0.0,
                                  ALU.add, ALU.max).then_inc(dve_h2, 1)

            def mlp3(t):
                pass

            dve.memset(warm[:, :], 0.0).then_inc(warm_set, 1)
            prepare_hot(0)
            prepare_hot(1)
            dve.memset(pair[:, :, :, :], 0.0).then_inc(zeroed, 1)
            steps = {"hot": hot, "turn": turn, "gram": gram, "early": early, "late": late, "mlp1": mlp1,
                     "mlp1_early": mlp1_early, "mlp1_late": mlp1_late, "mlp2": mlp2, "mlp3": mlp3}
            for name, *args in ORDER:
                steps[name](*args)


def kernel(**inputs):
    import concourse.bacc as bacc
    from concourse.bass_utils import run_bass_kernel_spmd

    a = {k: np.asarray(v) for k, v in inputs.items()}
    w1 = a["W_top1"]
    w1_pairs = np.zeros((P, PAIR_CHUNKS, H1), np.float32)
    for right in range(1, SLOTS):
        c, k = divmod(right - 1, QUADS)
        for left in range(right):
            w1_pairs[k * QUAD + left, c] = w1[pair_row(SLOT_FEATURE[left], SLOT_FEATURE[right])]
    w1_list = np.zeros((P, LIST_CHUNKS, H1), np.float32)
    for left in range(SIDE):
        for right in range(left, SIDE):
            chunk, at = divmod(list_row(left, right), P)
            w1_list[at, chunk] = w1[pair_row(SLOT_FEATURE[left], SLOT_FEATURE[right + 1])]
    ids = a["ids"].reshape(TILES, P, N_TABLES)
    arrays = {
        "dense_t": a["r_dense_features"].T,
        "ids": ids[:, :, GATHERED].transpose(1, 0, 2),
        "hot_ids": a["ids"][:, HOT_TABLES].T,
        "w1_pairs": w1_pairs,
        "w1_list": w1_list,
        "w1_dense": np.stack([w1[0:D], w1[-D:]], axis=1),
        "w2": a["W_top2"],
        "w3": a["W_top3"].reshape(H2_TILES, P).T,
        "b1": a["b_top1"].reshape(H1_TILES, P).T,
        "b2": a["b_top2"].reshape(H2_TILES, P).T,
        "ident": np.eye(P, dtype=np.float32),
        "hot_row": np.arange(P * HOT_CHUNKS, dtype=np.float32).reshape(P, HOT_CHUNKS),
    }
    arrays |= {f"tbl_{t}": a[f"tbl_{t}"] for t in range(N_TABLES)}
    arrays = {k: np.ascontiguousarray(v) for k, v in arrays.items()}

    nc = bacc.Bacc("TRN2", target_bir_lowering=False, num_devices=1)
    aps = {k: nc.dram_tensor(k, v.shape, mybir.dt.from_np(v.dtype), kind="ExternalInput").ap()
           for k, v in arrays.items()}
    gram_dram = nc.dram_tensor("gram_dram", (FIRST_DIRECT, LIST_ROWS, P), F32).ap()
    y = nc.dram_tensor("y", (BATCH, 1), F32, kind="ExternalOutput").ap()
    build(nc, aps["dense_t"], aps["ids"], aps["hot_ids"], [aps[f"tbl_{t}"] for t in GATHERED],
          [aps[f"tbl_{t}"] for t in HOT_TABLES], aps["w1_pairs"], aps["w1_list"], aps["w1_dense"], aps["w2"], aps["w3"],
          aps["b1"], aps["b2"], aps["ident"], aps["hot_row"], gram_dram, y.rearrange("b o -> o b"))
    r = run_bass_kernel_spmd(nc, [arrays], core_ids=[0])
    return r.results[0]["y"]
```

```python
from contextlib import ExitStack

import concourse.bass as bass
import numpy as np
from concourse import mybir

ALU = mybir.AluOpType
ACT = mybir.ActivationFunctionType
F32 = mybir.dt.float32
BF16 = mybir.dt.bfloat16
F16 = mybir.dt.float16
I32 = mybir.dt.int32
U32 = mybir.dt.uint32

P = 128
D = 128
BATCH = 512
TILES = BATCH // P
N_TABLES = 26
HOT_TABLES = [3, 6, 7, 13, 14, 15, 17, 24]
N_HOT = len(HOT_TABLES)
MIXED = N_HOT - 1
MIXED_FROM = 2
GATHERED = [HOT_TABLES[MIXED]] + [t for t in range(N_TABLES) if t not in HOT_TABLES]
N_GATHERED = len(GATHERED)
SLOTS = N_TABLES + 1
FIRST_GATHERED = 1 + MIXED
SLOT_FEATURE = [0] + [1 + t for t in HOT_TABLES[:MIXED]] + [1 + t for t in GATHERED]

HOT_ROWS = 1000
HOT_CHUNKS = 8
HOT_PARTS = HOT_ROWS // HOT_CHUNKS
HALF_TABLE = HOT_CHUNKS * D // 2

SIDE = SLOTS - 1
QUADS = 4
QUAD = 32
GROUPS = P // QUADS
UNITS = 2
UNIT_GROUPS = GROUPS // UNITS
LAST = TILES - 1


def pair_blocks():
    blocks, first = [], 0
    while first < SIDE:
        end = min(SIDE, first + P // (SIDE - first))
        blocks.append((first, end))
        first = end
    return blocks


BLOCKS = pair_blocks()
CHUNKS = len(BLOCKS)
BLOCK_ROWS = [(end - first) * (SIDE - first) for first, end in BLOCKS]

H1, H2 = 512, 256
WARM_UP = 11
H1_TILES, H2_TILES = H1 // P, H2 // P

SET = 4
SET_OF = [(i, min(i + SET, N_GATHERED)) for i in range(0, N_GATHERED, SET)]
SETS = len(SET_OF)

ORDER = [
    ("hot", 0), ("hot", 1), ("turn", 0, 0), ("hot", 2), ("turn", 0, 1), ("hot", 3), ("turn", 0, 2), ("hot", 4),
    ("turn", 0, 3), ("turn", 0, 4), ("hot", 5), ("turn", 1, 0), ("turn", 1, 1), ("turn", 1, 2), ("hot", 6),
    ("turn", 1, 3), ("turn", 1, 4), ("gram", 0, 0), ("gram", 0, 1), ("gram", 1, 0), ("gram", 1, 1),
    ("turn", 2, 0), ("turn", 2, 1), ("hot", 7), ("dense", 0), ("turn", 2, 2), ("mlp1", 0), ("turn", 2, 3),
    ("mlp2", 0), ("turn", 2, 4), ("dense", 1), ("gram", 2, 0), ("gram", 2, 1), ("mlp1", 1), ("turn", 3, 0),
    ("turn", 3, 1), ("mlp2", 1), ("dense", 2), ("turn", 3, 2), ("mlp1", 2), ("turn", 3, 3), ("turn", 3, 4),
    ("mlp3", 0), ("gram", 3, 0), ("gram", 3, 1), ("mlp2", 2), ("dense", 3), ("keep", 8, 8, 3), ("mlp1", 3),
    ("mlp2", 3), ("mlp3", 1),
]


def hot_from(i):
    return MIXED_FROM * P if i == MIXED else 0


def tables_of(t, q):
    first, end = SET_OF[q]
    return (max(first, 1), end) if t >= MIXED_FROM else (first, end)


def dve_turns(at):
    return at > SETS and at % 2 == 1


def pair_row(a, b):
    a, b = min(a, b), max(a, b)
    return D + a * (SLOTS - 1) - a * (a - 1) // 2 + (b - a - 1)


def build(nc, dense_t, ids, hot_ids, tables, hot_tables, w1_pairs, w1_dense, w2, w3, b1, b2, ident, hot_row, y):
    with ExitStack() as ctx:
        def sb(name, shape, dt):
            return ctx.enter_context(nc.sbuf_tensor(name, shape, dt))

        def psum(name, shape, dt=F32):
            return ctx.enter_context(nc.psum_tensor(name, shape, dt))

        def sem(name):
            return ctx.enter_context(nc.semaphore(name))

        vec = sb("vec", [P, BATCH, SLOTS], F32)
        rows = sb("rows", [P, 2, N_GATHERED, D], F32)
        ids_sb = sb("ids_sb", [P, TILES, N_GATHERED], I32)
        hot_ids_sb = sb("hot_ids_sb", [HOT_PARTS, 2, BATCH], I32)
        hot_ids_f = sb("hot_ids_f", [HOT_PARTS, 2, BATCH], F16)
        one_hot = sb("one_hot", [HOT_PARTS, 2, HOT_CHUNKS, BATCH], BF16)
        table = sb("table", [HOT_PARTS, 3, HOT_CHUNKS * D], F32)
        rest1 = sb("rest1", [HOT_PARTS, 2, HOT_CHUNKS * D], F32)
        rest2 = sb("rest2", [HOT_PARTS, 2, HOT_CHUNKS * D], F32)
        gram_sb = sb("gram_sb", [SIDE, 2, SIDE, P], F32)
        pair = sb("pair", [P, 2, CHUNKS, P], F32)
        warm = sb("warm", [P, BATCH], BF16)
        dense_sb = sb("dense_sb", [P, BATCH], F32)
        w1p = sb("w1p", [P, CHUNKS, H1], F32)
        w1d = sb("w1d", [P, 2, H1], F32)
        w1s = w1d[:, 0, :]
        w2_sb = sb("w2_sb", [P, H1_TILES, H2], F32)
        small = sb("small", [P, H2_TILES + H1_TILES + H2_TILES], F32)
        w3_sb = small[:, 0:H2_TILES]
        b1_sb = small[:, H2_TILES:H2_TILES + H1_TILES]
        b2_sb = small[:, H2_TILES + H1_TILES:]
        ident_sb = sb("ident_sb", [P, P], F32)
        hot_row_sb = sb("hot_row_sb", [P, HOT_CHUNKS], F32)
        h1_sb = sb("h1_sb", [P, 2, H1_TILES, P], F32)
        h2_sb = sb("h2_sb", [P, H2_TILES, 2, P], F32)
        y_sb = sb("y_sb", [1, BATCH], F32)

        turn_ps = psum("turn_ps", [P, 2, 512])
        hot_ps = psum("hot_ps", [P, 2, BATCH])
        gram_ps = psum("gram_ps", [P, 2, 512])
        h1_ps = psum("h1_ps", [P, 2, 512])

        ids_in = sem("ids_in")
        hot_ids_in = [sem(f"hot_ids_in{i}") for i in range(N_HOT)]
        table_in = [sem(f"table_in{i}") for i in range(N_HOT)]
        hot_row_in = sem("hot_row_in")
        ident_in = sem("ident_in")
        dense_in = sem("dense_in")
        w1d_in = sem("w1d_in")
        w1p_in = sem("w1p_in")
        pairs_in = [[sem(f"pairs_in{t}_{c}") for c in range(CHUNKS)] for t in range(TILES)]
        mlp_in = sem("mlp_in")
        rows_in = [[sem(f"rows_in{t}_{q}") for q in range(SETS)] for t in range(TILES)]
        warm_set = sem("warm_set")
        dense_set = sem("dense_set")
        w1_summed = sem("w1_summed")
        ids_cast = sem("ids_cast")
        hot_ready = sem("hot_ready")
        rest1_ready = sem("rest1_ready")
        rest2_ready = sem("rest2_ready")
        hot_done = sem("hot_done")
        hot_out = sem("hot_out")
        turn_done = sem("turn_done")
        act_turned = sem("act_turned")
        dve_turned = sem("dve_turned")
        gram_done = sem("gram_done")
        act_pairs = sem("act_pairs")
        dve_pairs = sem("dve_pairs")
        h1_low_done = sem("h1_low_done")
        h1_high_done = sem("h1_high_done")
        act_h1 = sem("act_h1")
        dve_h1 = sem("dve_h1")
        h2_low_done = sem("h2_low_done")
        h2_high_done = sem("h2_high_done")
        act_h2 = sem("act_h2")
        dve_h2 = sem("dve_h2")
        mlp3_done = sem("mlp3_done")
        y_set = sem("y_set")
        y_stored = sem("y_stored")

        def sample_slots(t):
            return vec[:, t * P:(t + 1) * P, :].rearrange("d (j g) s -> d j g s", j=QUADS)

        def h1_tile(m):
            return h1_ps[:, m // 2, (m % 2) * P:(m % 2 + 1) * P]

        def h2_tile(m):
            return hot_ps[:, m, 0:P]

        y_row = hot_ps[0:1, 0, P:3 * P]

        def gram_slot(t, u):
            return (t * UNITS + u) % 2

        def turned(engine, n, of=None):
            if of is None or not dve_turns(of):
                engine.wait_ge(act_turned, sum(not dve_turns(i) for i in range(n)))
            if of is None or dve_turns(of):
                if any(dve_turns(i) for i in range(n)):
                    engine.wait_ge(dve_turned, sum(dve_turns(i) for i in range(n)))

        def turn_copy(copy, t, q):
            first, end = tables_of(t, q)
            return copy(vec[:, t * P:(t + 1) * P, FIRST_GATHERED + first:FIRST_GATHERED + end],
                        turn_ps[:, (t * SETS + q) % 2, 0:(end - first) * P].rearrange("d (n b) -> d b n", b=P))

        def pairs_moved(engine, t):
            for c in range(CHUNKS):
                engine.wait_ge(pairs_in[t][c], 16)

        def gram_copy(copy, t, u, j):
            src = gram_ps[QUAD * j:QUAD * j + SIDE, gram_slot(t, u), 0:UNIT_GROUPS * SIDE]
            at = j * GROUPS + u * UNIT_GROUPS
            return copy(gram_sb[:, t % 2, :, at:at + UNIT_GROUPS], src.rearrange("f (g r) -> f r g", r=SIDE))

        block = ctx.enter_context(nc.Block())

        @block.sync
        def _(sp):
            sp.dma_start(ids_sb[:, :, :], ids).then_inc(ids_in, 16)
            for i in range(N_HOT):
                if i >= 2:
                    sp.wait_ge(ids_cast, i - 1)
                sp.dma_start(hot_ids_sb[:, i % 2, :], hot_ids[i].partition_broadcast(HOT_PARTS)
                             ).then_inc(hot_ids_in[i], 16)
                if i >= 3:
                    sp.wait_ge(hot_done, i - 2)
                    sp.wait_ge(rest1_ready, 2 * (i - 2))
                sp.dma_start(table[:, i % 3, :], hot_tables[i].rearrange("(p c) d -> p (c d)", c=HOT_CHUNKS)
                             ).then_inc(table_in[i], 16)
                if i == 0:
                    sp.dma_start(ident_sb[:, :], ident).then_inc(ident_in, 16)
                if i == 2:
                    sp.dma_start(dense_sb[:, :], dense_t).then_inc(dense_in, 16)
                    sp.dma_start(w1d[:, :, :], w1_dense).then_inc(w1d_in, 16)
                    sp.dma_start(w1p[:, :, :], w1_pairs).then_inc(w1p_in, 16)
                    sp.dma_start(w2_sb[:, :, :], w2.rearrange("(c p) m -> p c m", p=P)).then_inc(mlp_in, 16)
                    sp.dma_start(small[:, 0:H2_TILES], w3).then_inc(mlp_in, 16)
                    sp.dma_start(small[:, H2_TILES:H2_TILES + H1_TILES], b1).then_inc(mlp_in, 16)
                    sp.dma_start(small[:, H2_TILES + H1_TILES:], b2).then_inc(mlp_in, 16)
            for t in range(TILES):
                sp.wait_ge(act_pairs, UNITS * (t + 1))
                sp.wait_ge(dve_pairs, UNITS * (t + 1))
                if t >= 2:
                    sp.wait_ge(h1_high_done, t - 1)
                for c, (first, end) in enumerate(BLOCKS):
                    sp.dma_start(pair[0:BLOCK_ROWS[c], t % 2, c, :], gram_sb[first:end, t % 2, first:SIDE, :]
                                 ).then_inc(pairs_in[t][c], 16)
            sp.wait_ge(y_set, TILES // 2)
            sp.dma_start(y, y_sb[:, :]).then_inc(y_stored, 16)
            sp.wait_ge(y_stored, 16)

        @block.gpsimd
        def _(pool):
            pool.wait_ge(ids_in, 16)
            for t in range(TILES):
                for q in range(SETS):
                    first, end = tables_of(t, q)
                    if t >= 2:
                        pool.wait_ge(turn_done, (t - 2) * SETS + q + 1)
                    for n in range(first, end):
                        pool.indirect_dma_start(
                            rows[:, t % 2, n, :], None, tables[n],
                            bass.IndirectOffsetOnAxis(ids_sb[:, t, n:n + 1].bitcast(U32), 0),
                        ).then_inc(rows_in[t][q], 16)

        @block.tensor
        def _(pe):
            def hot(i):
                start = hot_from(i)
                pe.wait_ge(table_in[i], 16)
                if i >= 2:
                    pe.wait_ge(hot_out, i - 1)
                parts = [table[:, i % 3], rest1[:, i % 2], rest2[:, i % 2]]
                ready = [None, rest1_ready, rest2_ready]
                for n in range(3):
                    high = parts[n].bitcast(BF16).rearrange("p (c d h) -> p c d h", d=D, h=2)[:, :, :, 1]
                    for c in range(HOT_CHUNKS):
                        if n == 0:
                            pe.wait_ge(hot_ready, i * HOT_CHUNKS + c + 1)
                        elif c * D % HALF_TABLE == 0:
                            pe.wait_ge(ready[n], 2 * i + c * D // HALF_TABLE + 1)
                        mm = pe.matmul(hot_ps[:, i % 2, start:], high[:, c, :], one_hot[:, i % 2, c, start:],
                                       start=(n == 0 and c == 0), stop=(n == 2 and c == HOT_CHUNKS - 1))
                mm.then_inc(hot_done, 1)

            def turn(t, q):
                first, end = tables_of(t, q)
                at = t * SETS + q
                if at == 0:
                    pe.wait_ge(ident_in, 16)
                pe.wait_ge(rows_in[t][q], 16 * (end - first))
                if at >= 2:
                    turned(pe, at - 1, at - 2)
                for n in range(first, end):
                    mm = pe.transpose(turn_ps[:, at % 2, (n - first) * P:(n - first + 1) * P], rows[:, t % 2, n, :],
                                      ident_sb[:, :])
                mm.then_inc(turn_done, 1)

            def grams_read(n):
                pe.wait_ge(act_pairs, n)
                pe.wait_ge(dve_pairs, n)

            def gram(t, u):
                turned(pe, (t + 1) * SETS)
                if t == 0:
                    pe.wait_ge(hot_out, MIXED)
                    pe.wait_ge(dense_set, 1)
                else:
                    grams_read(UNITS * (t - 1) + u + 1)
                if t == MIXED_FROM:
                    pe.wait_ge(hot_out, N_HOT)
                of = sample_slots(t)
                for g in range(UNIT_GROUPS):
                    for j in range(QUADS):
                        own = of[:, j, u * UNIT_GROUPS + g, :]
                        mm = pe.matmul(gram_ps[QUAD * j:QUAD * j + SIDE, gram_slot(t, u), g * SIDE:(g + 1) * SIDE],
                                       own[:, 0:SIDE], own[:, 1:SLOTS], start=True, stop=True)
                mm.then_inc(gram_done, 1)

            def dense(t):
                if t == 0:
                    pe.wait_ge(w1_summed, 1)
                else:
                    pe.wait_ge(act_h1, t)
                    pe.wait_ge(dve_h1, t)
                for m in range(H1_TILES):
                    pe.matmul(h1_tile(m), w1s[:, m * P:(m + 1) * P], dense_sb[:, t * P:(t + 1) * P],
                              start=(m % 2 == 0), stop=False, skip_group_check=True)

            def mlp1(t):
                if t == 0:
                    pe.wait_ge(w1p_in, 16)

                def add(m, c):
                    k = BLOCK_ROWS[c]
                    return pe.matmul(h1_tile(m), w1p[0:k, c, m * P:(m + 1) * P], pair[0:k, t % 2, c, :],
                                     start=False, stop=(c == CHUNKS - 1), skip_group_check=True)
                for c in range(CHUNKS - 2):
                    pe.wait_ge(pairs_in[t][c], 16)
                    for m in range(H1_TILES):
                        add(m, c)
                pe.wait_ge(pairs_in[t][CHUNKS - 2], 16)
                pe.wait_ge(pairs_in[t][CHUNKS - 1], 16)
                for m in range(H1_TILES):
                    add(m, CHUNKS - 2)
                    mm = add(m, CHUNKS - 1)
                    if m == 1:
                        mm.then_inc(h1_low_done, 1)
                mm.then_inc(h1_high_done, 1)

            def mlp2(t):
                if t == 0:
                    pe.wait_ge(mlp_in, 64)
                else:
                    pe.wait_ge(act_h2, t)
                    pe.wait_ge(dve_h2, t)
                    if t >= 2:
                        pe.wait_ge(y_set, t // 2)

                def add(m, c):
                    return pe.matmul(h2_tile(m), w2_sb[:, c, m * P:(m + 1) * P],
                                     h1_sb[:, t % 2, c, :], start=(c == 0), stop=(c == H1_TILES - 1))
                pe.wait_ge(act_h1, t + 1)
                for c in (0, 1):
                    add(0, c)
                    add(1, c)
                pe.wait_ge(dve_h1, t + 1)
                add(0, 2)
                add(0, 3).then_inc(h2_low_done, 1)
                add(1, 2)
                add(1, 3).then_inc(h2_high_done, 1)

            def mlp3(p):
                def add(c):
                    return pe.matmul(y_row, w3_sb[:, c:c + 1], h2_sb[:, c, :, :],
                                     start=(c == 0), stop=(c == H2_TILES - 1))
                pe.wait_ge(act_h2, 2 * (p + 1))
                add(0)
                pe.wait_ge(dve_h2, 2 * (p + 1))
                add(1).then_inc(mlp3_done, 1)

            def keep(n, hots, t):
                pe.wait_ge(hot_out, hots)
                if t:
                    pe.wait_ge(dve_h2, t)
                for _ in range(n):
                    pe.matmul(hot_ps[:, 1, 0:256], warm[:, 0:P], warm[:, 0:256], start=True, stop=True)

            pe.wait_ge(warm_set, 1)
            for _ in range(WARM_UP):
                pe.matmul(hot_ps[:, 1, :], warm[:, 0:P], warm[:, :], start=True, stop=True)
            steps = {"hot": hot, "turn": turn, "gram": gram, "dense": dense, "keep": keep, "mlp1": mlp1,
                     "mlp2": mlp2, "mlp3": mlp3}
            for name, *args in ORDER:
                steps[name](*args)

        @block.scalar
        def _(act):
            act.dma_start(hot_row_sb[:, :], hot_row).then_inc(hot_row_in, 16)

            def hot(i):
                act.wait_ge(hot_done, i + 1)
                act.copy(vec[:, hot_from(i):, 1 + i], hot_ps[:, i % 2, hot_from(i):]).then_inc(hot_out, 1)

            def turn(t, q):
                at = t * SETS + q
                if not dve_turns(at):
                    act.wait_ge(turn_done, at + 1)
                    turn_copy(act.copy, t, q).then_inc(act_turned, 1)

            def gram(t, u):
                act.wait_ge(gram_done, t * UNITS + u + 1)
                if t >= 2:
                    pairs_moved(act, t - 2)
                for j in (0, 1):
                    last = gram_copy(act.copy, t, u, j)
                last.then_inc(act_pairs, 1)

            def mlp1(t):
                act.wait_ge(h1_low_done, t + 1)
                if t == 0:
                    act.wait_ge(mlp_in, 64)
                if t >= 2:
                    act.wait_ge(h2_high_done, t - 1)
                for m in (0, 1):
                    last = act.activation(h1_sb[:, t % 2, m, :], h1_tile(m), ACT.Relu, bias=b1_sb[:, m:m + 1])
                last.then_inc(act_h1, 1)

            def dense(t):
                pass

            def keep(n, hots, t):
                pass

            def mlp2(t):
                act.wait_ge(h2_low_done, t + 1)
                if t >= 2:
                    act.wait_ge(mlp3_done, t // 2)
                act.activation(h2_sb[:, 0, t % 2, :], h2_tile(0), ACT.Relu, bias=b2_sb[:, 0:1]).then_inc(act_h2, 1)

            def mlp3(p):
                act.wait_ge(mlp3_done, p + 1)
                act.copy(y_sb[:, 2 * p * P:2 * (p + 1) * P], y_row).then_inc(y_set, 1)

            steps = {"hot": hot, "turn": turn, "gram": gram, "dense": dense, "keep": keep, "mlp1": mlp1,
                     "mlp2": mlp2, "mlp3": mlp3}
            for name, *args in ORDER:
                steps[name](*args)

        @block.vector
        def _(dve):

            def prepare_hot(i):
                start = hot_from(i)
                if i == 0:
                    dve.wait_ge(hot_row_in, 16)
                dve.wait_ge(hot_ids_in[i], 16)
                if i >= 2:
                    dve.wait_ge(hot_done, i - 1)
                dve.tensor_copy(hot_ids_f[:, i % 2, start:], hot_ids_sb[:, i % 2, start:]).then_inc(ids_cast, 1)
                dve.wait_ge(ids_cast, i + 1)
                for c in range(HOT_CHUNKS):
                    dve.tensor_scalar(one_hot[:, i % 2, c, start:], hot_ids_f[:, i % 2, start:],
                                      hot_row_sb[0:HOT_PARTS, c:c + 1], None, ALU.is_equal).then_inc(hot_ready, 1)
                dve.wait_ge(table_in[i], 16)
                for h in range(2):
                    half = table[:, i % 3, h * HALF_TABLE:(h + 1) * HALF_TABLE]
                    dve.tensor_tensor(rest1[:, i % 2, h * HALF_TABLE:(h + 1) * HALF_TABLE], half, high_half(half),
                                      ALU.subtract).then_inc(rest1_ready, 1)
                for h in range(2):
                    dve.wait_ge(rest1_ready, 2 * i + h + 1)
                    half = rest1[:, i % 2, h * HALF_TABLE:(h + 1) * HALF_TABLE]
                    dve.tensor_tensor(rest2[:, i % 2, h * HALF_TABLE:(h + 1) * HALF_TABLE], half, high_half(half),
                                      ALU.subtract).then_inc(rest2_ready, 1)

            def high_half(x):
                return x.bitcast(BF16).rearrange("p (n h) -> p n h", h=2)[:, :, 1]

            def hot(i):
                if i + 2 < N_HOT:
                    prepare_hot(i + 2)
                if i == 1:
                    dve.wait_ge(dense_in, 16)
                    dve.tensor_copy(vec[:, :, 0], dense_sb[:, :]).then_inc(dense_set, 1)
                    dve.wait_ge(w1d_in, 16)
                    dve.tensor_tensor(w1s[:, :], w1d[:, 0, :], w1d[:, 1, :], ALU.add).then_inc(w1_summed, 1)

            def turn(t, q):
                at = t * SETS + q
                if dve_turns(at):
                    dve.wait_ge(turn_done, at + 1)
                    turn_copy(dve.tensor_copy, t, q).then_inc(dve_turned, 1)

            def gram(t, u):
                dve.wait_ge(gram_done, t * UNITS + u + 1)
                if t >= 2:
                    pairs_moved(dve, t - 2)
                for j in (2, 3):
                    last = gram_copy(dve.tensor_copy, t, u, j)
                last.then_inc(dve_pairs, 1)

            def mlp1(t):
                dve.wait_ge(h1_high_done, t + 1)
                if t == 0:
                    dve.wait_ge(mlp_in, 64)
                if t >= 2:
                    dve.wait_ge(h2_high_done, t - 1)
                for m in (2, 3):
                    last = dve.tensor_scalar(h1_sb[:, t % 2, m, :], h1_tile(m), b1_sb[:, m:m + 1], 0.0,
                                             ALU.add, ALU.max)
                last.then_inc(dve_h1, 1)

            def dense(t):
                pass

            def keep(n, hots, t):
                pass

            def mlp2(t):
                dve.wait_ge(h2_high_done, t + 1)
                if t >= 2:
                    dve.wait_ge(mlp3_done, t // 2)
                dve.tensor_scalar(h2_sb[:, 1, t % 2, :], h2_tile(1), b2_sb[:, 1:2], 0.0,
                                  ALU.add, ALU.max).then_inc(dve_h2, 1)

            def mlp3(p):
                pass

            dve.memset(warm[:, :], 0.0).then_inc(warm_set, 1)
            prepare_hot(0)
            prepare_hot(1)
            steps = {"hot": hot, "turn": turn, "gram": gram, "dense": dense, "keep": keep, "mlp1": mlp1,
                     "mlp2": mlp2, "mlp3": mlp3}
            for name, *args in ORDER:
                steps[name](*args)


def kernel(**inputs):
    import concourse.bacc as bacc
    from concourse.bass_utils import run_bass_kernel_spmd

    a = {k: np.asarray(v) for k, v in inputs.items()}
    w1 = a["W_top1"]
    w1_pairs = np.zeros((P, CHUNKS, H1), np.float32)
    for c, (first, end) in enumerate(BLOCKS):
        for left in range(first, end):
            for right in range(left, SIDE):
                w1_pairs[(left - first) * (SIDE - first) + right - first, c] = w1[
                    pair_row(SLOT_FEATURE[left], SLOT_FEATURE[right + 1])]
    ids = a["ids"].reshape(TILES, P, N_TABLES)
    arrays = {
        "dense_t": a["r_dense_features"].T,
        "ids": ids[:, :, GATHERED].transpose(1, 0, 2),
        "hot_ids": a["ids"][:, HOT_TABLES].T,
        "w1_pairs": w1_pairs,
        "w1_dense": np.stack([w1[0:D], w1[-D:]], axis=1),
        "w2": a["W_top2"],
        "w3": a["W_top3"].reshape(H2_TILES, P).T,
        "b1": a["b_top1"].reshape(H1_TILES, P).T,
        "b2": a["b_top2"].reshape(H2_TILES, P).T,
        "ident": np.eye(P, dtype=np.float32),
        "hot_row": np.arange(P * HOT_CHUNKS, dtype=np.float32).reshape(P, HOT_CHUNKS),
    }
    arrays |= {f"tbl_{t}": a[f"tbl_{t}"] for t in range(N_TABLES)}
    arrays = {k: np.ascontiguousarray(v) for k, v in arrays.items()}

    nc = bacc.Bacc("TRN2", target_bir_lowering=False, num_devices=1)
    aps = {k: nc.dram_tensor(k, v.shape, mybir.dt.from_np(v.dtype), kind="ExternalInput").ap()
           for k, v in arrays.items()}
    y = nc.dram_tensor("y", (BATCH, 1), F32, kind="ExternalOutput").ap()
    build(nc, aps["dense_t"], aps["ids"], aps["hot_ids"], [aps[f"tbl_{t}"] for t in GATHERED],
          [aps[f"tbl_{t}"] for t in HOT_TABLES], aps["w1_pairs"], aps["w1_dense"], aps["w2"], aps["w3"],
          aps["b1"], aps["b2"], aps["ident"], aps["hot_row"], y.rearrange("b o -> o b"))
    r = run_bass_kernel_spmd(nc, [arrays], core_ids=[0])
    return r.results[0]["y"]
```
